# Optimizing a Trainium2 kernel written in Bass

```python
import numpy as np
import jax
import jax.numpy as jnp

def _softmax(x, axis=-1):
    return jax.nn.softmax(x, axis=axis)

def _gelu(x):
    return jax.nn.gelu(x, approximate=True)

def _silu(x):
    return jax.nn.silu(x)

def _sigmoid(x):
    return jax.nn.sigmoid(x)

def _layernorm(x, axis=-1, eps=1e-05):
    m = jnp.mean(x, axis=axis, keepdims=True)
    v = jnp.var(x, axis=axis, keepdims=True)
    return (x - m) / jnp.sqrt(v + eps)

def _scatter_add(tgt, idx, src, axis=0):
    return tgt.at[idx].add(src)

def _segment_sum(src, seg, n):
    return jax.ops.segment_sum(src, seg, n)
kernel_name = 'mk_dlrm_tower_d1_rec_r8_d70751'

def setup_inputs(seed: int=0):
    np.random.seed(seed)
    _w = jnp.asarray

    def _rec_inputs():
        import jax
        import jax.numpy as jnp
        _tk = jax.random.key(seed)
        dense_ctx = jax.random.normal(jax.random.fold_in(_tk, 190), (1024, 16), jnp.float32)
        ids = jnp.stack([jax.random.randint(jax.random.fold_in(_tk, 200 + f), (1024,), 0, v, jnp.int32) for f, v in enumerate([1250, 12500, 125000, 1000, 125000, 1250, 125000, 1250, 125000, 1000, 125000, 1250, 125000, 125000, 1250, 1250, 125000, 1000, 125000, 1000, 12500, 1000, 1000, 125000, 1250, 125000, 125000, 12500, 1250, 1000, 1250, 125000, 125000, 1250, 1250, 1000, 12500, 12500, 1250])], axis=1)
        tbl_0 = 0.05 * jax.random.normal(jax.random.fold_in(_tk, 500 + 0), (1250, 16), jnp.float32)
        tbl_1 = 0.05 * jax.random.normal(jax.random.fold_in(_tk, 500 + 1), (12500, 16), jnp.float32)
        tbl_2 = 0.05 * jax.random.normal(jax.random.fold_in(_tk, 500 + 2), (125000, 16), jnp.float32)
        tbl_3 = 0.05 * jax.random.normal(jax.random.fold_in(_tk, 500 + 3), (1000, 16), jnp.float32)
        tbl_4 = 0.05 * jax.random.normal(jax.random.fold_in(_tk, 500 + 4), (125000, 16), jnp.float32)
        tbl_5 = 0.05 * jax.random.normal(jax.random.fold_in(_tk, 500 + 5), (1250, 16), jnp.float32)
        tbl_6 = 0.05 * jax.random.normal(jax.random.fold_in(_tk, 500 + 6), (125000, 16), jnp.float32)
        tbl_7 = 0.05 * jax.random.normal(jax.random.fold_in(_tk, 500 + 7), (1250, 16), jnp.float32)
        tbl_8 = 0.05 * jax.random.normal(jax.random.fold_in(_tk, 500 + 8), (125000, 16), jnp.float32)
        tbl_9 = 0.05 * jax.random.normal(jax.random.fold_in(_tk, 500 + 9), (1000, 16), jnp.float32)
        tbl_10 = 0.05 * jax.random.normal(jax.random.fold_in(_tk, 500 + 10), (125000, 16), jnp.float32)
        tbl_11 = 0.05 * jax.random.normal(jax.random.fold_in(_tk, 500 + 11), (1250, 16), jnp.float32)
        tbl_12 = 0.05 * jax.random.normal(jax.random.fold_in(_tk, 500 + 12), (125000, 16), jnp.float32)
        tbl_13 = 0.05 * jax.random.normal(jax.random.fold_in(_tk, 500 + 13), (125000, 16), jnp.float32)
        tbl_14 = 0.05 * jax.random.normal(jax.random.fold_in(_tk, 500 + 14), (1250, 16), jnp.float32)
        tbl_15 = 0.05 * jax.random.normal(jax.random.fold_in(_tk, 500 + 15), (1250, 16), jnp.float32)
        tbl_16 = 0.05 * jax.random.normal(jax.random.fold_in(_tk, 500 + 16), (125000, 16), jnp.float32)
        tbl_17 = 0.05 * jax.random.normal(jax.random.fold_in(_tk, 500 + 17), (1000, 16), jnp.float32)
        tbl_18 = 0.05 * jax.random.normal(jax.random.fold_in(_tk, 500 + 18), (125000, 16), jnp.float32)
        tbl_19 = 0.05 * jax.random.normal(jax.random.fold_in(_tk, 500 + 19), (1000, 16), jnp.float32)
        tbl_20 = 0.05 * jax.random.normal(jax.random.fold_in(_tk, 500 + 20), (12500, 16), jnp.float32)
        tbl_21 = 0.05 * jax.random.normal(jax.random.fold_in(_tk, 500 + 21), (1000, 16), jnp.float32)
        tbl_22 = 0.05 * jax.random.normal(jax.random.fold_in(_tk, 500 + 22), (1000, 16), jnp.float32)
        tbl_23 = 0.05 * jax.random.normal(jax.random.fold_in(_tk, 500 + 23), (125000, 16), jnp.float32)
        tbl_24 = 0.05 * jax.random.normal(jax.random.fold_in(_tk, 500 + 24), (1250, 16), jnp.float32)
        tbl_25 = 0.05 * jax.random.normal(jax.random.fold_in(_tk, 500 + 25), (125000, 16), jnp.float32)
        tbl_26 = 0.05 * jax.random.normal(jax.random.fold_in(_tk, 500 + 26), (125000, 16), jnp.float32)
        tbl_27 = 0.05 * jax.random.normal(jax.random.fold_in(_tk, 500 + 27), (12500, 16), jnp.float32)
        tbl_28 = 0.05 * jax.random.normal(jax.random.fold_in(_tk, 500 + 28), (1250, 16), jnp.float32)
        tbl_29 = 0.05 * jax.random.normal(jax.random.fold_in(_tk, 500 + 29), (1000, 16), jnp.float32)
        tbl_30 = 0.05 * jax.random.normal(jax.random.fold_in(_tk, 500 + 30), (1250, 16), jnp.float32)
        tbl_31 = 0.05 * jax.random.normal(jax.random.fold_in(_tk, 500 + 31), (125000, 16), jnp.float32)
        tbl_32 = 0.05 * jax.random.normal(jax.random.fold_in(_tk, 500 + 32), (125000, 16), jnp.float32)
        tbl_33 = 0.05 * jax.random.normal(jax.random.fold_in(_tk, 500 + 33), (1250, 16), jnp.float32)
        tbl_34 = 0.05 * jax.random.normal(jax.random.fold_in(_tk, 500 + 34), (1250, 16), jnp.float32)
        tbl_35 = 0.05 * jax.random.normal(jax.random.fold_in(_tk, 500 + 35), (1000, 16), jnp.float32)
        tbl_36 = 0.05 * jax.random.normal(jax.random.fold_in(_tk, 500 + 36), (12500, 16), jnp.float32)
        tbl_37 = 0.05 * jax.random.normal(jax.random.fold_in(_tk, 500 + 37), (12500, 16), jnp.float32)
        tbl_38 = 0.05 * jax.random.normal(jax.random.fold_in(_tk, 500 + 38), (1250, 16), jnp.float32)
        _rk = jax.random.fold_in(_tk, 7)
        W_top1 = 0.0693375 * jax.random.normal(jax.random.fold_in(_tk, 801), (208, 512), jnp.float32)
        W_top2 = 0.0441942 * jax.random.normal(jax.random.fold_in(_tk, 802), (512, 256), jnp.float32)
        W_top3 = 0.0625 * jax.random.normal(jax.random.fold_in(_tk, 803), (256, 1), jnp.float32)
        b_top1 = jnp.zeros((512,), jnp.float32)
        b_top2 = jnp.zeros((256,), jnp.float32)
        return (dense_ctx, ids, tbl_0, tbl_1, tbl_2, tbl_3, tbl_4, tbl_5, tbl_6, tbl_7, tbl_8, tbl_9, tbl_10, tbl_11, tbl_12, tbl_13, tbl_14, tbl_15, tbl_16, tbl_17, tbl_18, tbl_19, tbl_20, tbl_21, tbl_22, tbl_23, tbl_24, tbl_25, tbl_26, tbl_27, tbl_28, tbl_29, tbl_30, tbl_31, tbl_32, tbl_33, tbl_34, tbl_35, tbl_36, tbl_37, tbl_38, W_top1, b_top1, W_top2, b_top2, W_top3)
    dense_ctx, ids, tbl_0, tbl_1, tbl_2, tbl_3, tbl_4, tbl_5, tbl_6, tbl_7, tbl_8, tbl_9, tbl_10, tbl_11, tbl_12, tbl_13, tbl_14, tbl_15, tbl_16, tbl_17, tbl_18, tbl_19, tbl_20, tbl_21, tbl_22, tbl_23, tbl_24, tbl_25, tbl_26, tbl_27, tbl_28, tbl_29, tbl_30, tbl_31, tbl_32, tbl_33, tbl_34, tbl_35, tbl_36, tbl_37, tbl_38, W_top1, b_top1, W_top2, b_top2, W_top3 = _rec_inputs()

    def _L0_rec_setup():
        import jax, jax.numpy as jnp
        import numpy as np
        key = jax.random.key(seed)
        k1, k2, k3 = jax.random.split(key, 3)
        B, F0, D = (1024, 39, 16)
        L = 128
        hash_x = jax.random.normal(k1, (B, F0, D), dtype=jnp.float32)
        W0 = jax.random.normal(k2, (F0 * F0, L), dtype=jnp.float32) * 0.05
        W1 = jax.random.normal(k3, (F0 * (L // 2), L), dtype=jnp.float32) * 0.05
        return {'hash_x': hash_x, 'W0': W0, 'W1': W1}
    _L0_rec_all = _L0_rec_setup()
    _L0_rec_in = {k: v for k, v in _L0_rec_all.items() if k in ('W0', 'W1')}
    del _L0_rec_all
    return {'dense_ctx': dense_ctx, 'ids': ids, 'tbl_0': tbl_0, 'tbl_1': tbl_1, 'tbl_2': tbl_2, 'tbl_3': tbl_3, 'tbl_4': tbl_4, 'tbl_5': tbl_5, 'tbl_6': tbl_6, 'tbl_7': tbl_7, 'tbl_8': tbl_8, 'tbl_9': tbl_9, 'tbl_10': tbl_10, 'tbl_11': tbl_11, 'tbl_12': tbl_12, 'tbl_13': tbl_13, 'tbl_14': tbl_14, 'tbl_15': tbl_15, 'tbl_16': tbl_16, 'tbl_17': tbl_17, 'tbl_18': tbl_18, 'tbl_19': tbl_19, 'tbl_20': tbl_20, 'tbl_21': tbl_21, 'tbl_22': tbl_22, 'tbl_23': tbl_23, 'tbl_24': tbl_24, 'tbl_25': tbl_25, 'tbl_26': tbl_26, 'tbl_27': tbl_27, 'tbl_28': tbl_28, 'tbl_29': tbl_29, 'tbl_30': tbl_30, 'tbl_31': tbl_31, 'tbl_32': tbl_32, 'tbl_33': tbl_33, 'tbl_34': tbl_34, 'tbl_35': tbl_35, 'tbl_36': tbl_36, 'tbl_37': tbl_37, 'tbl_38': tbl_38, 'W_top1': W_top1, 'b_top1': b_top1, 'W_top2': W_top2, 'b_top2': b_top2, 'W_top3': W_top3, 'L0_rec_W0': _L0_rec_in['W0'], 'L0_rec_W1': _L0_rec_in['W1']}

def reference(dense_ctx, ids, tbl_0, tbl_1, tbl_2, tbl_3, tbl_4, tbl_5, tbl_6, tbl_7, tbl_8, tbl_9, tbl_10, tbl_11, tbl_12, tbl_13, tbl_14, tbl_15, tbl_16, tbl_17, tbl_18, tbl_19, tbl_20, tbl_21, tbl_22, tbl_23, tbl_24, tbl_25, tbl_26, tbl_27, tbl_28, tbl_29, tbl_30, tbl_31, tbl_32, tbl_33, tbl_34, tbl_35, tbl_36, tbl_37, tbl_38, W_top1, b_top1, W_top2, b_top2, W_top3, L0_rec_W0, L0_rec_W1):
    import jax
    import jax.numpy as jnp

    def _L0_rec_ref(hash_x, W0, W1):
        import jax, jax.numpy as jnp
        import numpy as np
        x0 = hash_x
        B, F0, D = x0.shape
        L = W0.shape[1]
        z0 = jnp.einsum('bid,bjd->bdij', x0, x0).reshape(B, D, F0 * F0)
        cur0 = jax.nn.relu(jnp.einsum('bdk,kl->bld', z0, W0))
        next_h, direct0 = jnp.split(cur0, 2, axis=1)
        Fk = next_h.shape[1]
        z1 = jnp.einsum('bid,bjd->bdij', x0, next_h).reshape(B, D, F0 * Fk)
        cur1 = jax.nn.relu(jnp.einsum('bdk,kl->bld', z1, W1))
        result = jnp.concatenate([direct0, cur1], axis=1)
        return jnp.sum(result, axis=-1)
    e = jnp.stack([tbl_0[ids[:, 0]], tbl_1[ids[:, 1]], tbl_2[ids[:, 2]], tbl_3[ids[:, 3]], tbl_4[ids[:, 4]], tbl_5[ids[:, 5]], tbl_6[ids[:, 6]], tbl_7[ids[:, 7]], tbl_8[ids[:, 8]], tbl_9[ids[:, 9]], tbl_10[ids[:, 10]], tbl_11[ids[:, 11]], tbl_12[ids[:, 12]], tbl_13[ids[:, 13]], tbl_14[ids[:, 14]], tbl_15[ids[:, 15]], tbl_16[ids[:, 16]], tbl_17[ids[:, 17]], tbl_18[ids[:, 18]], tbl_19[ids[:, 19]], tbl_20[ids[:, 20]], tbl_21[ids[:, 21]], tbl_22[ids[:, 22]], tbl_23[ids[:, 23]], tbl_24[ids[:, 24]], tbl_25[ids[:, 25]], tbl_26[ids[:, 26]], tbl_27[ids[:, 27]], tbl_28[ids[:, 28]], tbl_29[ids[:, 29]], tbl_30[ids[:, 30]], tbl_31[ids[:, 31]], tbl_32[ids[:, 32]], tbl_33[ids[:, 33]], tbl_34[ids[:, 34]], tbl_35[ids[:, 35]], tbl_36[ids[:, 36]], tbl_37[ids[:, 37]], tbl_38[ids[:, 38]]], axis=1)
    z = _L0_rec_ref(e, L0_rec_W0, L0_rec_W1)
    z = z.reshape(z.shape[0], -1)
    h = jnp.concatenate([z, dense_ctx], axis=1)
    h = jnp.maximum(h @ W_top1 + b_top1, 0.0)
    h = jnp.maximum(h @ W_top2 + b_top2, 0.0)
    y = h @ W_top3
    return y

_drawn_inputs = setup_inputs


def setup_inputs(seed=0):
    import zlib

    import numpy as np

    out = dict(_drawn_inputs(seed))
    spreads = {'b_top1': (0.0, 0.8), 'b_top2': (0.0, 0.449)}
    factors = {'tbl_0': 8.0,
     'tbl_1': 8.0,
     'tbl_2': 8.0,
     'tbl_3': 8.0,
     'tbl_4': 8.0,
     'tbl_5': 8.0,
     'tbl_6': 8.0,
     'tbl_7': 8.0,
     'tbl_8': 8.0,
     'tbl_9': 8.0,
     'tbl_10': 8.0,
     'tbl_11': 8.0,
     'tbl_12': 8.0,
     'tbl_13': 8.0,
     'tbl_14': 8.0,
     'tbl_15': 8.0,
     'tbl_16': 8.0,
     'tbl_17': 8.0,
     'tbl_18': 8.0,
     'tbl_19': 8.0,
     'tbl_20': 8.0,
     'tbl_21': 8.0,
     'tbl_22': 8.0,
     'tbl_23': 8.0,
     'tbl_24': 8.0,
     'tbl_25': 8.0,
     'tbl_26': 8.0,
     'tbl_27': 8.0,
     'tbl_28': 8.0,
     'tbl_29': 8.0,
     'tbl_30': 8.0,
     'tbl_31': 8.0,
     'tbl_32': 8.0,
     'tbl_33': 8.0,
     'tbl_34': 8.0,
     'tbl_35': 8.0,
     'tbl_36': 8.0,
     'tbl_37': 8.0,
     'tbl_38': 8.0,
     'L0_rec_W1': 8.0}
    for name, (base, spread) in spreads.items():
        noise = np.random.default_rng([zlib.crc32(name.encode()), seed]).standard_normal(out[name].shape)
        drawn = base * np.exp(spread * noise) if base else spread * noise
        out[name] = jnp.asarray(drawn.astype(out[name].dtype))
    for name, factor in factors.items():
        out[name] = (out[name] * factor).astype(out[name].dtype)
    return out
```

```python
from contextlib import ExitStack

import numpy as np

import concourse.bass as bass
from concourse import mybir

ALU = mybir.AluOpType
ACT = mybir.ActivationFunctionType
AX = mybir.AxisListType
F32 = mybir.dt.float32
F32R = mybir.dt.float32r
BF16 = mybir.dt.bfloat16
I32 = mybir.dt.int32

P = 128
BATCH, FIELDS, DIM, MAPS = 1024, 39, 16, 128
NEXT = MAPS // 2
DENSE, TOP1, TOP2 = 16, 512, 256

BLOCKS = BATCH // P
HALVES = 2
TILES = BLOCKS * HALVES
DT = DIM // HALVES
COLS = DT * P
BANK = 512
NB = COLS // BANK

SHIFTS = FIELDS // 2 + 1
REP = 3
ROWS0 = REP * FIELDS
CH0 = -(-SHIFTS // REP)
CH1 = -(-FIELDS // 2)
PARTS = 3
SELS = CH0 + CH1 + 1
SEL_COPY = CH0 + CH1

TILE_EVENTS = "11T11A11" + "01" * CH0 + "1" * (CH1 - 6 - CH0)
LOOK = 5
HEAD_EVENTS = "TA" + "0" * CH0 + "-" * (LOOK + 1)
SUB_LAG = 2
NBUF = 6
RELU_LAG = LOOK
SUM_LAG = RELU_LAG + 2
POOL_SUBS = (13, 10)
GATHERS_ODD = 24
GATHER_SLOTS_ODD, GATHER_SLOTS_EVEN = 27, 18
SPLIT_AT = 21


def plan():
    events = []

    def add(kinds, tile):
        n = {"0": 0, "1": 0}
        for k in kinds:
            c = n.get(k, 0)
            if k in n:
                n[k] += 1
            events.append((k, tile if k == "1" else tile + 1, c))

    add(HEAD_EVENTS, -1)
    for t in range(TILES - 1):
        add(TILE_EVENTS, t)
    add("1" * CH1, TILES - 1)
    return events


def pairs():
    a = -np.ones((ROWS0, CH0), np.int64)
    b = -np.ones((ROWS0, CH0), np.int64)
    for s in range(SHIFTS):
        for f in range(FIELDS):
            g = (f + s) % FIELDS
            a[s % REP * FIELDS + f, s // REP] = f * FIELDS + g
            if s:
                b[s % REP * FIELDS + f, s // REP] = g * FIELDS + f
    return a, b


def selections():
    sel = np.zeros((PARTS, FIELDS, SELS, P), np.float32)
    for s in range(SHIFTS):
        for f in range(FIELDS):
            sel[:, (f + s) % FIELDS, s // REP, s % REP * FIELDS + f] = 1
    for f in range(FIELDS):
        sel[:, f, CH0 + f // 2, f % 2 * NEXT:f % 2 * NEXT + NEXT] = 1
        for r in range(REP):
            sel[:, f, SEL_COPY, r * FIELDS + f] = 1
    return sel.reshape(PARTS * FIELDS, SELS, P)


def build(nc, ids, tables, sel_in, w0a_in, w0b_in, w1_in, dense_in, top1_in, b1_in, top2_in, b2_in, top3_in, eye_in, out):
    events = plan()
    n_ev = len(events)
    head = len(HEAD_EVENTS)
    per_tile = len(TILE_EVENTS)
    per_block = HALVES * per_tile
    tile_at = [head + per_tile * t for t in range(TILES)]
    KR = PARTS * FIELDS

    steps_to, copies_to, dsubs_to, psubs_to, fills_to = [], [], [], [], []
    on_pool = []
    n = [0, 0, 0, 0, 0]
    for e, (kind, tile, c) in enumerate(events):
        step = kind in "01"
        at = (e - head) % per_tile
        par = (e - head) // per_tile % 2
        share = POOL_SUBS[par] if e >= head else CH0 - 3
        total = CH0 + CH1 if e >= head else CH0
        idx = sum(x in "01" for x in (TILE_EVENTS[:at] if e >= head else HEAD_EVENTS[:e]))
        if e >= tile_at[-1]:
            idx = e - tile_at[-1]
        pool = step and (idx * share) % total < share
        on_pool.append(pool)
        n[0] += step
        n[1] += kind in "TA"
        n[2] += step and not pool
        n[3] += pool
        n[4] += kind != "-"
        for k, to in enumerate((steps_to, copies_to, dsubs_to, psubs_to, fills_to)):
            to.append(n[k])

    def per_block_of(to):
        return to[tile_at[4]] - to[tile_at[2]]

    B_FILL, B_STEP, B_COPY = per_block_of(fills_to), per_block_of(steps_to), per_block_of(copies_to)
    B_DSUB, B_PSUB = per_block_of(dsubs_to), per_block_of(psubs_to)

    last0 = {}
    last1 = {}
    for e, (kind, tile, c) in enumerate(events):
        if kind == "0":
            last0[tile] = e
        if kind == "1":
            last1[tile] = e
    first = {}
    for e, (kind, tile, c) in enumerate(events):
        first.setdefault((kind, tile), e)

    with ExitStack() as ctx:
        def sb(name, shape, dt=F32):
            return ctx.enter_context(nc.sbuf_tensor(name, shape, dt))

        def sem(name):
            return ctx.enter_context(nc.semaphore(name))

        ids_now = sb("ids_now", [P, FIELDS], I32)
        rows = sb("rows", [P, FIELDS * DIM])
        rest = sb("rest", [P, DIM, FIELDS])
        parts = sb("parts", [P, DIM, PARTS, FIELDS], BF16)
        xparts = sb("xparts", [KR, 2, COLS], BF16)
        work = sb("work", [P, SELS * P])
        xcopy = work[0:ROWS0, 0:COLS]
        hid = sb("hid", [P, 2, COLS])
        direct = work[:, COLS:2 * COLS]
        cur = work[:, 2 * COLS:3 * COLS]
        z = sb("z", [P, NBUF, COLS])
        zh = sb("zh", [P, NBUF, COLS], F32R)
        zl = sb("zl", [P, NBUF, COLS], F32R)
        wh = sb("wh", [P, CH0 + CH1, MAPS], F32R)
        wl = sb("wl", [P, CH0 + CH1, MAPS], F32R)
        sel = sb("sel", [KR, SELS, P], BF16)
        eye = sb("eye", [P, P], BF16)
        part_d = sb("part_d", [P, 2, P])
        part_c = sb("part_c", [P, 2, P])
        feat_c = sb("feat_c", [P, BATCH])
        feat_d = sb("feat_d", [P, BATCH])
        top1 = sb("top1", [P, 2, TOP1])
        top2 = sb("top2", [P, TOP1 // P, TOP2])
        top3 = sb("top3", [P, TOP2 // P])
        b1 = sb("b1", [P, TOP1 // P])
        b2 = sb("b2", [P, TOP2 // P])
        y_row = sb("y_row", [1, BATCH])
        stage_w1 = z[:, 0:3, :].rearrange("p a c -> p (a c)")[:, 0:CH1 * MAPS]
        stage_w0a = z[:, 3, 0:CH0 * MAPS]
        stage_w0b = z[:, 4, 0:CH0 * MAPS]
        stage_sel = work[0:KR, :]
        stage_eye = z[:, 5, 0:P]
        act1 = z[:, 0:TOP1 // P, :]
        act2 = z[:, TOP1 // P:TOP1 // P + TOP2 // P, :]

        psum = ctx.enter_context(nc.psum_tensor("psum", [P, 8, BANK], F32))
        slot = [psum[:, NB * s:NB * s + NB, :] for s in range(2)]
        acc = [psum[:, 4 + NB * s:4 + NB * s + NB, :] for s in range(2)]

        ids_loaded = sem("ids_loaded")
        w_loaded = sem("w_loaded")
        sel_loaded = sem("sel_loaded")
        top_loaded = sem("top_loaded")
        gathered = sem("gathered")
        split = sem("split")
        setup_v = sem("setup_v")
        w_ready = sem("w_ready")
        sel_ready = sem("sel_ready")
        filled = sem("filled")
        copied = sem("copied")
        multiplied = sem("multiplied")
        rounded = sem("rounded")
        low_v = sem("low_v")
        low_p = sem("low_p")
        summed = sem("summed")
        hid_ready = sem("hid_ready")
        direct_ready = sem("direct_ready")
        cur_ready = sem("cur_ready")
        direct_used = sem("direct_used")
        cur_used = sem("cur_used")
        feats = sem("feats")
        top1_mm = sem("top1_mm")
        top1_act = sem("top1_act")
        top2_mm = sem("top2_mm")
        top2_act = sem("top2_act")
        top3_mm = sem("top3_mm")
        y_ready = sem("y_ready")
        stored = sem("stored")

        block = ctx.enter_context(nc.Block())
        loop_from, loop_to = 1, BLOCKS - 2

        def timeline(engine, slots_of, before=None):
            for e in range(-LOOK, tile_at[2]):
                slots_of(e, 0)
            with engine.Fori(0, loop_to - loop_from) as i:
                for e in range(tile_at[2], tile_at[4]):
                    slots_of(e, i)
            for e in range(tile_at[2 * loop_to], n_ev + SUM_LAG + 4):
                slots_of(e, 0)

        def ev(e):
            return events[e] if 0 <= e < n_ev else (None, None, None)

        def block_of(e):
            t = -1 if e < head else min((e - head) // per_tile, TILES - 1)
            at = e if e < head else e - tile_at[t]
            return t % 2, at, (t - t % 2) // 2

        @block.sync
        def _(sp):
            def load_ids(b):
                sp.dma_start(ids_now[:], ids[b]).then_inc(ids_loaded, 16)

            load_ids(0)
            sp.dma_start(stage_sel, sel_in).then_inc(sel_loaded, 16)
            sp.dma_start(stage_eye, eye_in).then_inc(sel_loaded, 16)
            sp.dma_start(stage_w0a[0:ROWS0], w0a_in).then_inc(w_loaded, 16)
            sp.dma_start(stage_w0b[0:ROWS0], w0b_in).then_inc(w_loaded, 16)
            sp.dma_start(stage_w1, w1_in).then_inc(w_loaded, 16)
            sp.dma_start(top1[:], top1_in).then_inc(top_loaded, 16)
            sp.dma_start(top2[:], top2_in).then_inc(top_loaded, 16)
            sp.dma_start(top3[:], top3_in).then_inc(top_loaded, 16)
            sp.dma_start(b1[:], b1_in).then_inc(top_loaded, 16)
            sp.dma_start(b2[:], b2_in).then_inc(top_loaded, 16)
            sp.wait_ge(setup_v, 1)
            sp.dma_start(feat_d[0:DENSE, :], dense_in).then_inc(top_loaded, 16)
            with sp.Fori(1, BLOCKS) as b:
                sp.wait_ge(gathered, b * (16 * FIELDS))
                sp.dma_start(ids_now[:], ids[bass.ds(b, 1)].rearrange("a p f -> (a p) f")).then_inc(ids_loaded, 16)
            sp.wait_ge(y_ready, NB)
            sp.dma_start(out, y_row[:]).then_inc(stored, 16)
            sp.wait_ge(stored, 16)

        @block.gpsimd
        def _(pool):
            def gather(f):
                pool.indirect_dma_start(rows[:, f * DIM:(f + 1) * DIM], None, tables[f],
                                        bass.IndirectOffsetOnAxis(ap=ids_now[:, f:f + 1], axis=0)).then_inc(gathered, 16)

            def slots_of(e, i):
                odd, at, b = block_of(e)
                if e < 0:
                    return
                slots, lo, hi, blk = ((GATHER_SLOTS_ODD, 0, GATHERS_ODD, b + 2) if odd else
                                      (GATHER_SLOTS_EVEN, GATHERS_ODD, FIELDS, b + 1))
                start = 1
                if e < head:
                    slots, start = head - 1, 0
                if odd and at == start and blk < BLOCKS:
                    pool.wait_ge(ids_loaded, 16 * (blk + 1) + i * 16)
                    pool.wait_ge(split, 4 * blk - 2 + i * 4)
                s = e - 1
                if 0 <= s < n_ev and on_pool[s]:
                    k = (steps_to[s] - 1) % NBUF
                    r = ROWS0 if events[s][0] == "0" else P
                    pool.wait_ge(rounded, steps_to[s] + i * B_STEP)
                    pool.tensor_tensor(zl[0:r, k, :], z[0:r, k, :], zh[0:r, k, :].bitcast(F32),
                                       ALU.subtract).then_inc(low_p, 1)
                if blk < BLOCKS and start <= at < start + slots:
                    n = at - start
                    for f in range(lo + (hi - lo) * n // slots, lo + (hi - lo) * (n + 1) // slots):
                        gather(f)

            pool.wait_ge(ids_loaded, 16)
            for f in range(FIELDS):
                gather(f)
            timeline(pool, slots_of)

        @block.vector
        def _(dve):
            rows_df = rows[:].rearrange("p (f d) -> p d f", d=DIM)

            def split_rows(n, b, i):
                if n == 0:
                    dve.wait_ge(gathered, 16 * FIELDS * (b + 1) + i * (16 * FIELDS))
                    if b > 0:
                        dve.wait_ge(filled, fills_to[first["T", 2 * b - 1]] + i * B_FILL)
                else:
                    dve.wait_ge(split, 4 * b + n + i * 4)
                if n == 0:
                    ins = dve.tensor_copy(parts[:, :, 0, :], rows_df)
                elif n == 1:
                    ins = dve.tensor_tensor(rest[:], rows_df, parts[:, :, 0, :], ALU.subtract)
                elif n == 2:
                    ins = dve.tensor_copy(parts[:, :, 1, :], rest[:])
                else:
                    ins = dve.tensor_tensor(parts[:, :, 2, :], rest[:], parts[:, :, 1, :], ALU.subtract)
                ins.then_inc(split, 1)

            def multiply(e, i):
                kind, tile, c = events[e]
                k = (steps_to[e] - 1) % NBUF
                if steps_to[e] > NBUF:
                    o = max(x for x in range(e) if steps_to[x] == steps_to[e] - NBUF and events[x][0] in "01")
                    if on_pool[o]:
                        dve.wait_ge(low_p, psubs_to[o] + i * B_PSUB)
                    else:
                        dve.wait_ge(low_v, dsubs_to[o] + i * B_DSUB)
                if kind == "0":
                    if c == 0:
                        dve.wait_ge(copied, copies_to[first["A", tile]] + i * B_COPY)
                    dve.wait_ge(filled, fills_to[e] + i * B_FILL)
                    src, other, to = slot[e % 2][0:ROWS0], xcopy, z[0:ROWS0, k, :]
                else:
                    if c == 0:
                        dve.wait_ge(hid_ready, tile + 1 + i * HALVES)
                    dve.wait_ge(filled, fills_to[e] + i * B_FILL)
                    src, other, to = slot[e % 2], hid[:, tile % 2, :], z[:, k, :]
                dve.tensor_tensor(to, src.rearrange("p a b -> p (a b)"), other, ALU.mult).then_inc(multiplied, 1)

            def low(e, i):
                k = (steps_to[e] - 1) % NBUF
                r = ROWS0 if events[e][0] == "0" else P
                dve.wait_ge(rounded, steps_to[e] + i * B_STEP)
                dve.tensor_tensor(zl[0:r, k, :], z[0:r, k, :], zh[0:r, k, :].bitcast(F32), ALU.subtract).then_inc(low_v, 1)

            def sum_dims(src, part, feat, lo, tile, i, ready, used, n):
                dve.wait_ge(ready, tile + 1 + i * HALVES)
                if tile >= 2:
                    dve.wait_ge(feats, 2 * (tile // 2 - 1) + n + 1 + i * 2)
                dve.tensor_reduce(part[lo:P, tile % 2, :], src[lo:P, :].rearrange("p (d b) -> p b d", d=DT),
                                  AX.X, ALU.add).then_inc(used, 1)
                if tile % 2:
                    dve.wait_ge(used, tile + 1 + i * HALVES)
                    at = tile // 2 * P
                    to = feat[lo:P, at:at + P] if isinstance(i, int) else feat[lo:P, bass.ds(at + i * P, P)]
                    dve.tensor_tensor(to, part[lo:P, 0, :], part[lo:P, 1, :], ALU.add).then_inc(feats, 1)

            def slots_of(e, i):
                odd, at, b = block_of(e)
                if 0 <= e < n_ev and events[e][0] in "01":
                    multiply(e, i)
                s = e - SUB_LAG
                if 0 <= s < n_ev and events[s][0] in "01" and not on_pool[s]:
                    low(s, i)
                if e >= head and not odd and b + 1 < BLOCKS and SPLIT_AT <= at < SPLIT_AT + 4:
                    split_rows(at - SPLIT_AT, b + 1, i)
                for tile, last in last0.items():
                    if last + SUM_LAG == e:
                        sum_dims(direct, part_d, feat_d, NEXT, tile, i, direct_ready, direct_used, 0)
                for tile, last in last1.items():
                    if last + SUM_LAG == e:
                        sum_dims(cur, part_c, feat_c, 0, tile, i, cur_ready, cur_used, 1)

            dve.memset(feat_d[0:NEXT, :], 0.0).then_inc(setup_v, 1)
            split_rows(0, 0, 0)
            split_rows(1, 0, 0)
            split_rows(2, 0, 0)
            split_rows(3, 0, 0)
            dve.wait_ge(sel_loaded, 32)
            dve.tensor_copy(sel[:].rearrange("p s m -> p (s m)"), stage_sel)
            dve.tensor_copy(eye[:], stage_eye).then_inc(sel_ready, 1)
            dve.wait_ge(w_loaded, 48)
            w0h = wh[0:ROWS0, 0:CH0, :].rearrange("p c m -> p (c m)")
            w0l = wl[0:ROWS0, 0:CH0, :].rearrange("p c m -> p (c m)")
            w1h = wh[:, CH0:CH0 + CH1, :].rearrange("p c m -> p (c m)")
            w1l = wl[:, CH0:CH0 + CH1, :].rearrange("p c m -> p (c m)")
            dve.tensor_tensor(stage_w0a[0:ROWS0], stage_w0a[0:ROWS0], stage_w0b[0:ROWS0], ALU.add).then_inc(setup_v, 1)
            dve.wait_ge(setup_v, 2)
            dve.tensor_copy(w0h, stage_w0a[0:ROWS0])
            dve.tensor_copy(w1h, stage_w1).then_inc(setup_v, 1)
            dve.wait_ge(setup_v, 3)
            dve.tensor_tensor(w0l, stage_w0a[0:ROWS0], w0h.bitcast(F32), ALU.subtract)
            dve.tensor_tensor(w1l, stage_w1, w1h.bitcast(F32), ALU.subtract).then_inc(w_ready, 1)
            dve.wait_ge(w_ready, 1)
            timeline(dve, slots_of)
            dve.wait_ge(top3_mm, 1)
            for n in range(NB):
                dve.wait_ge(top3_mm, n + 1)
                dve.tensor_copy(y_row[:, n * BANK:(n + 1) * BANK], psum[0:1, 4 + n, :]).then_inc(y_ready, 1)

        @block.scalar
        def _(act):
            def copy_out(e, i):
                kind, tile, c = events[e]
                act.wait_ge(filled, fills_to[e] + i * B_FILL)
                if kind == "T":
                    src = slot[e % 2][0:KR].rearrange("p a b -> p (a b)").bitcast(BF16)[:, 0:COLS]
                    act.copy(xparts[:, tile % 2, :], src).then_inc(copied, 1)
                else:
                    act.copy(xcopy, slot[e % 2][0:ROWS0].rearrange("p a b -> p (a b)")).then_inc(copied, 1)

            def round_high(e, i):
                k = (steps_to[e] - 1) % NBUF
                r = ROWS0 if events[e][0] == "0" else P
                act.wait_ge(multiplied, steps_to[e] + i * B_STEP)
                if steps_to[e] > NBUF:
                    act.wait_ge(summed, steps_to[e] - NBUF + i * B_STEP)
                act.copy(zh[0:r, k, :], z[0:r, k, :]).then_inc(rounded, 1)

            def relu0(tile, i):
                a = acc[tile % 2].rearrange("p a b -> p (a b)")
                act.wait_ge(summed, steps_to[last0[tile]] + i * B_STEP)
                if tile >= 1:
                    act.wait_ge(direct_used, tile + i * HALVES)
                act.activation(direct[NEXT:P, :], a[NEXT:P], ACT.Relu).then_inc(direct_ready, 1)
                act.activation(hid[0:NEXT, tile % 2, :], a[0:NEXT], ACT.Relu)
                act.activation(hid[NEXT:P, tile % 2, :], a[0:NEXT], ACT.Relu).then_inc(hid_ready, 1)

            def relu1(tile, i):
                act.wait_ge(summed, steps_to[last1[tile]] + i * B_STEP)
                if tile >= 1:
                    act.wait_ge(cur_used, tile + i * HALVES)
                act.activation(cur, acc[tile % 2].rearrange("p a b -> p (a b)"), ACT.Relu).then_inc(cur_ready, 1)

            def slots_of(e, i):
                if 0 <= e < n_ev:
                    if events[e][0] in "01":
                        round_high(e, i)
                    elif events[e][0] in "TA":
                        copy_out(e, i)
                for tile, last in last0.items():
                    if last + RELU_LAG == e:
                        relu0(tile, i)
                for tile, last in last1.items():
                    if last + RELU_LAG == e:
                        relu1(tile, i)

            act.wait_ge(w_ready, 1)
            timeline(act, slots_of)
            act.wait_ge(top_loaded, 6 * 16)
            for n in range(NB):
                for m in range(TOP1 // P):
                    act.wait_ge(top1_mm, n * (TOP1 // P) + m + 1)
                    act.activation(act1[:, m, n * BANK:(n + 1) * BANK], psum[:, n * 4 + m, :], ACT.Relu,
                                   bias=b1[:, m:m + 1]).then_inc(top1_act, 1)
            for n in range(NB):
                for m in range(TOP2 // P):
                    act.wait_ge(top2_mm, n * (TOP2 // P) + m + 1)
                    act.activation(act2[:, m, n * BANK:(n + 1) * BANK], psum[:, n * 2 + m, :], ACT.Relu,
                                   bias=b2[:, m:m + 1]).then_inc(top2_act, 1)

        @block.tensor
        def _(pe):
            def fill(e, i):
                kind, tile, c = events[e]
                uses = [x for x in range(e % 2, e, 2) if events[x][0] != "-"]
                if uses and events[uses[-1]][0] in "01":
                    pe.wait_ge(multiplied, steps_to[uses[-1]] + i * B_STEP)
                elif uses:
                    pe.wait_ge(copied, copies_to[uses[-1]] + i * B_COPY)
                to = slot[e % 2]
                if kind == "T":
                    pe.wait_ge(split, 4 * (tile // 2) + 4 + i * 4)
                    flat = to[0:KR].rearrange("p a b -> p (a b)").bitcast(BF16)
                    for d in range(DT):
                        src = parts[:, tile % 2 * DT + d, :, :].rearrange("p r f -> p (r f)")
                        ins = pe.transpose(flat[:, d * P:(d + 1) * P], src, eye[:])
                    ins.then_inc(filled, 1)
                    return
                if kind == "A":
                    pe.wait_ge(copied, copies_to[first["T", tile]] + i * B_COPY)
                m = P if kind == "1" else ROWS0
                s = {"0": c, "1": CH0 + c, "A": SEL_COPY}[kind]
                for n in range(NB):
                    ins = pe.matmul(to[0:m, n, :], sel[:, s, 0:m], xparts[:, tile % 2, n * BANK:(n + 1) * BANK],
                                    start=True, stop=True)
                ins.then_inc(filled, 1)

            def product(e, i):
                kind, tile, c = events[e]
                k = (steps_to[e] - 1) % NBUF
                r = ROWS0 if kind == "0" else P
                w = c if kind == "0" else CH0 + c
                chunks = CH0 if kind == "0" else CH1
                a = acc[tile % 2]
                if c == 0 and kind == "0" and tile >= 2:
                    pe.wait_ge(cur_ready, tile - 1 + i * HALVES)
                if c == 0 and kind == "1":
                    pe.wait_ge(hid_ready, tile + 1 + i * HALVES)
                pe.wait_ge(rounded, steps_to[e] + i * B_STEP)
                for j, (w_, z_) in enumerate(((wh, zh), (wl, zh), (wh, zl))):
                    if j == 2:
                        if on_pool[e]:
                            pe.wait_ge(low_p, psubs_to[e] + i * B_PSUB)
                        else:
                            pe.wait_ge(low_v, dsubs_to[e] + i * B_DSUB)
                    for n in range(NB):
                        ins = pe.matmul(a[:, n, :], w_[0:r, w, :], z_[0:r, k, n * BANK:(n + 1) * BANK],
                                        start=(c == 0 and j == 0), stop=(c == chunks - 1 and j == 2))
                ins.then_inc(summed, 1)

            def slots_of(e, i):
                if 0 <= e < n_ev and events[e][0] in "01":
                    product(e, i)
                if 0 <= e + LOOK < n_ev and events[e + LOOK][0] != "-":
                    fill(e + LOOK, i)

            pe.wait_ge(sel_ready, 1)
            pe.wait_ge(w_ready, 1)
            timeline(pe, slots_of)
            pe.wait_ge(top_loaded, 6 * 16)
            pe.wait_ge(feats, 2 * BLOCKS)
            pe.wait_ge(cur_ready, TILES)
            pe.wait_ge(multiplied, steps_to[-1])
            for n in range(NB):
                for m in range(TOP1 // P):
                    for q, f in enumerate((feat_c, feat_d)):
                        ins = pe.matmul(psum[:, n * 4 + m, :], top1[:, q, m * P:(m + 1) * P],
                                        f[:, n * BANK:(n + 1) * BANK], start=(q == 0), stop=(q == 1))
                    ins.then_inc(top1_mm, 1)
            for n in range(NB):
                pe.wait_ge(top1_act, (n + 1) * (TOP1 // P))
                for m in range(TOP2 // P):
                    for q in range(TOP1 // P):
                        ins = pe.matmul(psum[:, n * 2 + m, :], top2[:, q, m * P:(m + 1) * P],
                                        act1[:, q, n * BANK:(n + 1) * BANK], start=(q == 0), stop=(q == TOP1 // P - 1))
                    ins.then_inc(top2_mm, 1)
            for n in range(NB):
                pe.wait_ge(top2_act, (n + 1) * (TOP2 // P))
                for q in range(TOP2 // P):
                    ins = pe.matmul(psum[0:1, 4 + n, :], top3[:, q:q + 1], act2[:, q, n * BANK:(n + 1) * BANK],
                                    start=(q == 0), stop=(q == TOP2 // P - 1))
                ins.then_inc(top3_mm, 1)


def kernel(**inputs):
    import concourse.bacc as bacc
    from concourse.bass_utils import run_bass_kernel_spmd

    nc = bacc.Bacc("TRN2", target_bir_lowering=False, num_devices=1)
    arrays = {}

    def given(name, a):
        a = np.ascontiguousarray(a)
        arrays[name] = a
        return nc.dram_tensor(name, a.shape, mybir.dt.from_np(a.dtype), kind="ExternalInput").ap()

    def rows_of(w, index):
        w = np.concatenate([w, np.zeros((1, w.shape[1]), w.dtype)])
        return w[index].reshape(index.shape[0], -1)

    w0 = np.asarray(inputs["L0_rec_W0"])
    w1 = np.asarray(inputs["L0_rec_W1"])
    a, b = pairs()
    w1_at = np.arange(CH1)[None, :] * P + np.arange(P)[:, None]
    w1_at[w1_at >= FIELDS * NEXT] = -1
    t1 = np.asarray(inputs["W_top1"])
    top1 = np.zeros((P, 2, TOP1), t1.dtype)
    top1[:, 0] = t1[NEXT:NEXT + MAPS]
    top1[NEXT:, 1] = t1[0:NEXT]
    top1[0:DENSE, 1] = t1[NEXT + MAPS:]
    args = [
        given("ids_dram", np.asarray(inputs["ids"]).reshape(BLOCKS, P, FIELDS)),
        [given(f"tbl_{f}_dram", np.asarray(inputs[f"tbl_{f}"])) for f in range(FIELDS)],
        given("sel_dram", selections().reshape(PARTS * FIELDS, SELS * P)),
        given("w0a_dram", rows_of(w0, a)),
        given("w0b_dram", rows_of(w0, b)),
        given("w1_dram", rows_of(w1, w1_at)),
        given("dense_dram", np.asarray(inputs["dense_ctx"]).T),
        given("top1_dram", top1),
        given("b1_dram", np.asarray(inputs["b_top1"]).reshape(-1, P).T),
        given("top2_dram", np.asarray(inputs["W_top2"]).reshape(-1, P, TOP2).transpose(1, 0, 2)),
        given("b2_dram", np.asarray(inputs["b_top2"]).reshape(-1, P).T),
        given("top3_dram", np.asarray(inputs["W_top3"]).reshape(-1, P).T),
        given("eye_dram", np.eye(P, dtype=np.float32)),
        nc.dram_tensor("y_dram", (1, BATCH), F32, kind="ExternalOutput").ap(),
    ]
    build(nc, *args)
    r = run_bass_kernel_spmd(nc, [arrays], core_ids=[0])
    return r.results[0]["y_dram"].reshape(BATCH, 1)
```

```python
from contextlib import ExitStack

import numpy as np

import concourse.bass as bass
from concourse import mybir

ALU = mybir.AluOpType
ACT = mybir.ActivationFunctionType
AX = mybir.AxisListType
F32 = mybir.dt.float32
F32R = mybir.dt.float32r
BF16 = mybir.dt.bfloat16
I32 = mybir.dt.int32

P = 128
BATCH, FIELDS, DIM, MAPS = 1024, 39, 16, 128
NEXT = MAPS // 2
DENSE, TOP1, TOP2 = 16, 512, 256

BLOCKS = BATCH // P
QUARTERS = 4
TILES = BLOCKS * QUARTERS
DT = DIM // QUARTERS
BANK = 512
COLS = DT * P
PAIR = 2
WIDE = PAIR * COLS

SHIFTS = FIELDS // 2 + 1
REP = 3
ROWS0 = REP * FIELDS
CH0 = -(-SHIFTS // REP)
CH1 = -(-FIELDS // 2)
PARTS = 3
SELS = CH0 + CH1
STEPS0 = -(-CH0 // PAIR)

BLOCK_EVENTS = ("1D01T0110110D11", "1D01101M011T0D11", "1DN0110110110D1T", "1D0110110110D1T")
FIRST_EVENTS = ("1D1011010101D1T", "PDM0110101110D1T")
LAST_EVENTS = ("1D0P1011011T0D1", "1D01101M1011T0D1", "1D01N1011011T0D1", "1101101101DT0D1",
               "1D0P10110110TD1", "1D01101M10110TD1", "1D01NP01P01PT0D1", "1D0P10PP01PT0D1")
AHEAD = {"1": 0, "P": 0, "D": 0, "0": 2, "Z": 2, "T": 3}
LAYER0, LAYER1, TOWER = "0Z", "1PD", "MNY"
RING = 4
LOOK = 3
PE_LOW_LAG = 1
HEAD_EVENTS = [("T", 0), ("T", 1)] + [("Z", 0)] * STEPS0 + [("Z", 1)] * STEPS0 + [("T", 2)]
TAIL_EVENTS = [("-", None)] * 6 + [(k, BLOCKS - 1) for k in TOWER]
SLOTS = 3
NBUF = 7
NSQ = 4
NKEPT = 4
STORE_LAG = 2
LEAD = 5
LOW_LAG = 1
RELU_LAG = 3
HEAD_RELU_LAG = 1
SUM_LAG = RELU_LAG + 2
GATHER_FIRST = 21
FIRST_TABLES = 28
GATHER_REST = 15
SPLIT_AT = 18
MOST = 36


def layer_of(kind):
    return "1" if kind in LAYER1 else "0" if kind in LAYER0 else kind


def plan():
    events, done = [], {}
    tiles = FIRST_EVENTS + BLOCK_EVENTS[len(FIRST_EVENTS):] + BLOCK_EVENTS * (BLOCKS - 3) + LAST_EVENTS

    def add(kind, at):
        if kind in AHEAD and at >= TILES:
            return
        if kind in TOWER and at < 0:
            kind = "-"
        layer = layer_of(kind)
        n = done.get((layer, at), 0)
        done[layer, at] = n + 1
        events.append((kind, at, PAIR * n))

    for kind, tile in HEAD_EVENTS:
        add(kind, tile)
    for t in range(TILES):
        for kind in tiles[t]:
            add(kind, t // QUARTERS - 1 if kind in TOWER else t + AHEAD[kind])
    for kind, b in TAIL_EVENTS:
        add(kind, b)
    return events


def spread_steps():
    found = set()
    for kinds in FIRST_EVENTS + BLOCK_EVENTS + LAST_EVENTS:
        steps = [k for k in kinds if k in LAYER1]
        found |= {n for n, k in enumerate(steps) if k == "D"}
    return sorted(found)


def pairs():
    a = -np.ones((ROWS0, CH0), np.int64)
    b = -np.ones((ROWS0, CH0), np.int64)
    for s in range(SHIFTS):
        for f in range(FIELDS):
            g = (f + s) % FIELDS
            a[s % REP * FIELDS + f, s // REP] = f * FIELDS + g
            if s:
                b[s % REP * FIELDS + f, s // REP] = g * FIELDS + f
    return a, b


def selections():
    sel = np.zeros((PARTS, FIELDS, SELS, P), np.float32)
    for s in range(SHIFTS):
        for f in range(FIELDS):
            for g in (f, (f + s) % FIELDS):
                sel[:, g, s // REP, s % REP * FIELDS + f] = 1
    for f in range(FIELDS):
        sel[:, f, CH0 + f // 2, f % 2 * NEXT:f % 2 * NEXT + NEXT] = 1
    return sel.reshape(PARTS * FIELDS, SELS, P)


def own_squares():
    fold = np.zeros((ROWS0, CH0, FIELDS), np.float32)
    for s in range(SHIFTS):
        for f in range(FIELDS):
            for g in {f, (f + s) % FIELDS}:
                fold[s % REP * FIELDS + f, s // REP, g] = -1 if s else 2
    return fold


def build(nc, ids, tables, sel_in, fold_in, w0a_in, w0b_in, w1_in, dense_in, top1_in, b1_in, top2_in, b2_in,
          top3_in, eye_in, out):
    events = plan()
    n_ev = len(events)
    head = len(HEAD_EVENTS)
    per_block = sum(map(len, BLOCK_EVENTS))
    block_at = [head + per_block * b for b in range(BLOCKS)]
    KR = PARTS * FIELDS
    SPREAD = spread_steps()
    FIELDS_STEP = 2 * PAIR
    NF = FIELDS_STEP * len(SPREAD)
    assert all(step * FIELDS_STEP >= MOST or (step + 1) * FIELDS_STEP <= MOST for step in SPREAD)

    counted = {"fills": "T1P" + LAYER0 + TOWER, "slots": "T1P" + LAYER0 + TOWER, "steps": LAYER0 + LAYER1,
               "copies": "T", "steps0": LAYER0, "steps1": LAYER1, "kept": "PD", "low_v": "1Z", "low_p": "0PD"}
    upto = {}
    for name, kinds in counted.items():
        n, upto[name] = 0, []
        for kind, _, _ in events:
            n += kind in kinds
            upto[name].append(n)
    a_block = {name: to[block_at[2]] - to[block_at[1]] for name, to in upto.items()}
    assert not (a_block["slots"] % SLOTS or a_block["steps"] % NBUF or a_block["steps0"] % NSQ or a_block["kept"] % NKEPT)

    def through(name, e, i):
        return upto[name][e] + i * a_block[name]

    first, last = {}, {}
    for e, (kind, tile, c) in enumerate(events):
        layer = layer_of(kind)
        first.setdefault((layer, tile), e)
        last[layer, tile] = e

    first_spread = min(e for e, event in enumerate(events) if event[0] == "D")
    last_spread = {tile: e for e, (kind, tile, _) in enumerate(events) if kind == "D"}

    def buf(e):
        return (upto["steps"][e] - 1) % NBUF

    def sq(e):
        return (upto["steps0"][e] - 1) % NSQ

    def kept(e):
        return (upto["kept"][e] - 1) % NKEPT

    def slot_of(e):
        return slot[(upto["slots"][e] - 1) % SLOTS]

    def user_before(e, name, back):
        n = upto[name][e] - back
        return None if n < 1 else upto[name].index(n)

    with ExitStack() as ctx:
        def sb(name, shape, dt=F32):
            return ctx.enter_context(nc.sbuf_tensor(name, shape, dt))

        def sem(name):
            return ctx.enter_context(nc.semaphore(name))

        ids_now = sb("ids_now", [P, FIELDS], I32)
        rows = sb("rows", [P, FIELDS * DIM])
        rows_kept = sb("rows_kept", [P, DIM, NF])
        xrows = sb("xrows", [NF, RING, COLS])
        rest = sb("rest", [P, DIM, FIELDS])
        parts = sb("parts", [P, DIM, PARTS, FIELDS], BF16)
        xparts = sb("xparts", [KR, RING, COLS], BF16)
        hid = sb("hid", [P, RING, COLS])
        maps = sb("maps", [P, 2, QUARTERS, COLS])
        squares = sb("squares", [P, NSQ, WIDE])
        products = sb("products", [P, NKEPT, WIDE])
        zh = sb("zh", [P, NBUF, WIDE], F32R)
        zl = sb("zl", [P, NBUF, WIDE], F32R)
        wh = sb("wh", [P, SELS, MAPS], F32R)
        wl = sb("wl", [P, SELS, MAPS], F32R)
        sel = sb("sel", [KR, SELS, P], BF16)
        fold = sb("fold", [ROWS0, CH0, FIELDS])
        eye = sb("eye", [P, P], BF16)
        eye_f = sb("eye_f", [P, P])
        warm = sb("warm", [P, 1])
        feat_c = sb("feat_c", [P, P])
        feat_d = sb("feat_d", [P, P])
        act1 = sb("act1", [P, TOP1 // P, P])
        act2 = sb("act2", [P, TOP2 // P, P])
        top1 = sb("top1", [P, 2, TOP1])
        top2 = sb("top2", [P, TOP1 // P, TOP2])
        top3 = sb("top3", [P, TOP2 // P])
        b1 = sb("b1", [P, TOP1 // P])
        b2 = sb("b2", [P, TOP2 // P])
        y_row = sb("y_row", [1, P + BATCH])
        x_dram = nc.dram_tensor("x_dram", (RING, 2, NF // 2, COLS), F32, kind="Internal").ap()
        stage_sel = maps[:].rearrange("p a q c -> p (a q c)")[0:KR, 0:SELS * P]
        stage_w1 = squares[:].rearrange("p a c -> p (a c)")[:, 0:CH1 * MAPS]
        stage_w0a = squares[:].rearrange("p a c -> p (a c)")[0:ROWS0, CH1 * MAPS:SELS * MAPS]
        stage_w0b = products[:, 0, 0:CH0 * MAPS][0:ROWS0]

        psum = ctx.enter_context(nc.psum_tensor("psum", [P, 8, BANK], F32))
        slot = [psum[:, PAIR * s:PAIR * s + PAIR, :] for s in range(SLOTS)]
        acc = [psum[:, SLOTS * PAIR + s, :] for s in range(2)]

        ids_loaded = sem("ids_loaded")
        w_loaded = sem("w_loaded")
        sel_loaded = sem("sel_loaded")
        top_loaded = sem("top_loaded")
        gathered_most = sem("gathered_most")
        gathered = sem("gathered")
        split_most = sem("split_most")
        split = sem("split")
        setup_v = sem("setup_v")
        spread = [sem(f"spread{n}") for n in range(NKEPT)]
        x_stored = [sem(f"x_stored{n}") for n in range(RING)]
        dense_loaded = sem("dense_loaded")
        folded = sem("folded")
        w_ready = sem("w_ready")
        sel_ready = sem("sel_ready")
        filled = sem("filled")
        copied = sem("copied")
        squared = sem("squared")
        multiplied = sem("multiplied")
        rounded = sem("rounded")
        low_v = sem("low_v")
        low_p = sem("low_p")
        summed = sem("summed")
        hid_ready = sem("hid_ready")
        direct_ready = sem("direct_ready")
        cur_ready = sem("cur_ready")
        direct_feats = sem("direct_feats")
        cur_feats = sem("cur_feats")
        top1_act = sem("top1_act")
        top2_act = sem("top2_act")
        y_ready = sem("y_ready")
        stored = sem("stored")

        block = ctx.enter_context(nc.Block())
        loop_from, loop_to = 1, BLOCKS - 2

        def timeline(engine, slots_of):
            for e in range(-max(LOOK, LEAD), block_at[loop_from]):
                slots_of(e, 0)
            with engine.Fori(0, loop_to - loop_from) as i:
                for e in range(block_at[loop_from], block_at[loop_from + 1]):
                    slots_of(e, i)
            for e in range(block_at[loop_to], n_ev + SUM_LAG):
                slots_of(e, 0)

        def wait_low(engine, e, i):
            if events[e][0] in "1Z":
                engine.wait_ge(low_v, through("low_v", e, i))
            else:
                engine.wait_ge(low_p, through("low_p", e, i))

        def spreads(e):
            return sum(events[x][0] == "D" and kept(x) == kept(e) for x in range(e + 1))

        def rows_in(b):
            return 16 * (FIELDS * (b + 1) - MOST)

        def kind_of(e):
            return events[e][0] if 0 <= e < n_ev else None

        def place_of(e):
            return (e - head) // per_block, (e - head) % per_block

        @block.sync
        def _(sp):
            def spread_x(e, i):
                _, tile, c = events[e]
                was = user_before(e, "kept", NKEPT)
                if was is not None:
                    wait_low(sp, was, i)
                if e == first_spread:
                    sp.wait_ge(x_stored[0], 16)
                row = FIELDS_STEP * SPREAD.index(c // PAIR)
                for half in range(2):
                    if half and e == last_spread[tile] and tile + 1 < TILES:
                        sp.wait_ge(x_stored[(tile + 1) % RING], 16 * ((tile + 1) // RING + 1) + i * 16)
                    src = x_dram[tile % RING, half, row // 2:row // 2 + PAIR, :]
                    sp.dma_start(products[half * NEXT:half * NEXT + NEXT, kept(e), :].rearrange("p (n c) -> p n c", n=PAIR),
                                 src.partition_broadcast(NEXT)).then_inc(spread[kept(e)], 16)

            def store_x(e, i):
                tile = events[e][1]
                sp.wait_ge(copied, through("copies", e, i))
                sp.dma_start(x_dram[tile % RING].rearrange("h n c -> (h n) c"),
                             xrows[:, tile % RING, :]).then_inc(x_stored[tile % RING], 16)

            def load_ids(b, i):
                src = ids[b] if isinstance(i, int) else ids[bass.ds(b + i, 1)].rearrange("a p f -> (a p) f")
                sp.dma_start(ids_now[:], src).then_inc(ids_loaded, 16)

            def load_dense(b, i):
                src = dense_in[b] if isinstance(i, int) else dense_in[bass.ds(b + i, 1)].rearrange("a d n -> (a d) n")
                sp.dma_start(feat_d[0:DENSE, :], src).then_inc(dense_loaded, 16)

            def slots_of(e, i):
                b, at = place_of(e)
                if kind_of(e + LEAD) == "D":
                    spread_x(e + LEAD, i)
                if kind_of(e - STORE_LAG) == "T":
                    store_x(e - STORE_LAG, i)
                if e >= head and at == GATHER_FIRST - 3 and b + 2 < BLOCKS:
                    sp.wait_ge(gathered, rows_in(b + 1) + i * (16 * FIELDS))
                    load_ids(b + 2, i)
                if kind_of(e - 1) == "M" and events[e - 1][1] + 1 < BLOCKS:
                    sp.wait_ge(filled, through("fills", e - 1, i))
                    load_dense(events[e - 1][1] + 1, i)

            load_ids(0, 0)
            sp.dma_start(stage_w0a, w0a_in).then_inc(w_loaded, 16)
            sp.dma_start(stage_w0b, w0b_in).then_inc(w_loaded, 16)
            sp.dma_start(fold[:], fold_in).then_inc(w_loaded, 16)
            sp.dma_start(stage_w1, w1_in).then_inc(w_loaded, 16)
            sp.dma_start(stage_sel, sel_in).then_inc(sel_loaded, 16)
            sp.dma_start(eye_f[:], eye_in).then_inc(sel_loaded, 16)
            sp.dma_start(top1[:], top1_in).then_inc(top_loaded, 16)
            sp.dma_start(top2[:], top2_in).then_inc(top_loaded, 16)
            sp.dma_start(top3[:], top3_in).then_inc(top_loaded, 16)
            sp.dma_start(b1[:], b1_in).then_inc(top_loaded, 16)
            sp.dma_start(b2[:], b2_in).then_inc(top_loaded, 16)
            sp.wait_ge(setup_v, 1)
            load_dense(0, 0)
            sp.wait_ge(gathered_most, 16 * MOST)
            sp.wait_ge(gathered, rows_in(0))
            load_ids(1, 0)
            timeline(sp, slots_of)
            sp.wait_ge(y_ready, BLOCKS + 1)
            sp.dma_start(out, y_row[:, P:]).then_inc(stored, 16)
            sp.wait_ge(stored, 16)

        @block.gpsimd
        def _(pool):
            def gather(f, signal):
                pool.indirect_dma_start(rows[:, f * DIM:(f + 1) * DIM], None, tables[f],
                                        bass.IndirectOffsetOnAxis(ap=ids_now[:, f:f + 1], axis=0)).then_inc(signal, 16)

            def gather_share(tables_, n, of):
                k = len(tables_)
                for f in tables_[k * n // of:k * (n + 1) // of]:
                    gather(f, gathered)

            def slots_of(e, i):
                if e < 0:
                    return
                b, at = place_of(e)
                start = GATHER_FIRST if e >= head else per_block - head
                if at == start and b + 2 < BLOCKS:
                    pool.wait_ge(ids_loaded, 16 * (b + 3) + i * 16)
                    pool.wait_ge(split, 4 * (b + 1) + 2 + i * 4)
                s = e - LOW_LAG
                if kind_of(s) == "0":
                    pool.wait_ge(squared, through("steps0", s, i))
                    k, q, w = buf(s), sq(s), COLS * min(PAIR, CH0 - events[s][2])
                    pool.tensor_tensor(zl[0:ROWS0, k, 0:w], squares[0:ROWS0, q, 0:w],
                                       zh[0:ROWS0, k, 0:w].bitcast(F32), ALU.subtract).then_inc(low_p, 1)
                if kind_of(s) in ("P", "D"):
                    pool.wait_ge(rounded, through("steps1", s, i))
                    pool.tensor_tensor(zl[:, buf(s), :], products[:, kept(s), :], zh[:, buf(s), :].bitcast(F32),
                                       ALU.subtract).then_inc(low_p, 1)
                if at >= start and b + 2 < BLOCKS:
                    gather_share(range(FIRST_TABLES), at - start, per_block - start)
                if at < GATHER_REST and 0 <= b < BLOCKS - 1:
                    gather_share(range(FIRST_TABLES, FIELDS), at, GATHER_REST)

            pool.wait_ge(ids_loaded, 16)
            for f in range(FIELDS):
                gather(f, gathered_most if f < MOST else gathered)
            timeline(pool, slots_of)

        @block.vector
        def _(dve):
            rows_df = rows[:].rearrange("p (f d) -> p d f", d=DIM)

            def split_step(n, f0, f1):
                src, left = rows_df[:, :, f0:f1], rest[:, :, f0:f1]
                if n == 0:
                    for k, step in enumerate(SPREAD):
                        lo, hi = step * FIELDS_STEP, (step + 1) * FIELDS_STEP
                        if f0 <= lo and hi <= f1:
                            to = rows_kept[:].rearrange("p d (h n) -> p d n h", h=2)[:, :, k * PAIR:(k + 1) * PAIR, :]
                            dve.tensor_copy(to, rows_df[:, :, lo:hi].rearrange("p d (n h) -> p d n h", h=2))
                    return dve.tensor_copy(parts[:, :, 0, f0:f1], src)
                if n == 1:
                    return dve.tensor_tensor(left, src, parts[:, :, 0, f0:f1], ALU.subtract)
                if n == 2:
                    return dve.tensor_copy(parts[:, :, 1, f0:f1], left)
                return dve.tensor_tensor(parts[:, :, 2, f0:f1], left, parts[:, :, 1, f0:f1], ALU.subtract)

            def split_first_rows():
                dve.wait_ge(gathered_most, 16 * MOST)
                for n in range(4):
                    if n > 0:
                        dve.wait_ge(split_most, n)
                    split_step(n, 0, MOST).then_inc(split_most, 1)
                dve.wait_ge(gathered, rows_in(0))
                for n in range(4):
                    if n > 0:
                        dve.wait_ge(split, n)
                    split_step(n, MOST, FIELDS).then_inc(split, 1)

            def split_rows(n, b, i):
                if n == 0:
                    dve.wait_ge(gathered, rows_in(b) + i * (16 * FIELDS))
                    dve.wait_ge(filled, through("fills", first["T", QUARTERS * b - 1], i))
                else:
                    dve.wait_ge(split, 4 * b + n + i * 4)
                split_step(n, 0, FIELDS).then_inc(split, 1)

            def multiply(e, i):
                kind, tile, c = events[e]
                if c == 0:
                    dve.wait_ge(hid_ready, tile + 1 + i * QUARTERS)
                to = products[:, kept(e), :].rearrange("p (a b) -> p a b", a=PAIR)
                if kind == "D":
                    src = to
                    dve.wait_ge(spread[kept(e)], 32 * spreads(e) + i * (32 * a_block["kept"] // NKEPT))
                else:
                    src = slot_of(e)
                    dve.wait_ge(filled, through("fills", e, i))
                    if kind == "1":
                        to = src
                    elif user_before(e, "kept", NKEPT) is not None:
                        wait_low(dve, user_before(e, "kept", NKEPT), i)
                dve.tensor_tensor(to, src, hid[:, tile % RING:tile % RING + 1, :].to_broadcast([P, PAIR, COLS]),
                                  ALU.mult).then_inc(multiplied, 1)

            def low0(e, i):
                dve.wait_ge(squared, through("steps0", e, i))
                w = COLS * min(PAIR, CH0 - events[e][2])
                dve.tensor_tensor(zl[0:ROWS0, buf(e), 0:w], squares[0:ROWS0, sq(e), 0:w],
                                  zh[0:ROWS0, buf(e), 0:w].bitcast(F32), ALU.subtract).then_inc(low_v, 1)

            def low(e, i):
                dve.wait_ge(rounded, through("steps1", e, i))
                dve.tensor_tensor(zl[:, buf(e), :], slot_of(e).rearrange("p a b -> p (a b)"),
                                  zh[:, buf(e), :].bitcast(F32), ALU.subtract).then_inc(low_v, 1)

            def sum_dims(which, feat, lo, b, i, ready, feats):
                dve.wait_ge(ready, QUARTERS * (b + 1) + i * QUARTERS)
                if b > 0:
                    dve.wait_ge(filled, through("fills", first["M", b - 1], i))
                dve.tensor_reduce(feat[lo:P, :], maps[lo:P, which].rearrange("p q (d b) -> p b (q d)", d=DT),
                                  AX.X, ALU.add).then_inc(feats, 1)

            def slots_of(e, i):
                b, at = place_of(e)
                if kind_of(e) in ("1", "P", "D"):
                    multiply(e, i)
                if kind_of(e - LOW_LAG) == "1":
                    low(e - LOW_LAG, i)
                if kind_of(e - LOW_LAG) == "Z":
                    low0(e - LOW_LAG, i)
                if e >= head and b + 1 < BLOCKS and SPLIT_AT <= at < SPLIT_AT + 4:
                    split_rows(at - SPLIT_AT, b + 1, i)
                for c in range(BLOCKS):
                    if last["0", QUARTERS * c + QUARTERS - 1] + SUM_LAG == e:
                        sum_dims(0, feat_d, NEXT, c, i, direct_ready, direct_feats)
                    if last["1", QUARTERS * c + QUARTERS - 1] + SUM_LAG == e:
                        sum_dims(1, feat_c, 0, c, i, cur_ready, cur_feats)

            dve.memset(act2[:], 0.0).then_inc(top2_act, 1)
            dve.memset(feat_d[0:NEXT, :], 0.0).then_inc(setup_v, 1)
            w0h = wh[0:ROWS0, 0:CH0, :].rearrange("p c m -> p (c m)")
            w0l = wl[0:ROWS0, 0:CH0, :].rearrange("p c m -> p (c m)")
            w1h = wh[:, CH0:SELS, :].rearrange("p c m -> p (c m)")
            w1l = wl[:, CH0:SELS, :].rearrange("p c m -> p (c m)")
            dve.wait_ge(w_loaded, 64)
            dve.tensor_tensor(stage_w0a, stage_w0a, stage_w0b, ALU.add).then_inc(setup_v, 1)
            dve.wait_ge(setup_v, 2)
            dve.tensor_scalar(stage_w0a, stage_w0a, 0.5, None, ALU.mult).then_inc(setup_v, 1)
            dve.wait_ge(sel_loaded, 32)
            dve.tensor_copy(sel[:].rearrange("p s m -> p (s m)"), stage_sel)
            dve.tensor_copy(eye[:], eye_f[:]).then_inc(sel_ready, 1)
            dve.wait_ge(folded, 1)
            dve.tensor_copy(stage_w0a[0:FIELDS, 0:MAPS], acc[0][0:FIELDS, 0:MAPS]).then_inc(setup_v, 1)
            dve.wait_ge(setup_v, 4)
            dve.tensor_copy(w0h, stage_w0a)
            dve.tensor_copy(w1h, stage_w1).then_inc(setup_v, 1)
            dve.wait_ge(setup_v, 5)
            dve.tensor_tensor(w0l, stage_w0a, w0h.bitcast(F32), ALU.subtract)
            dve.tensor_tensor(w1l, stage_w1, w1h.bitcast(F32), ALU.subtract).then_inc(w_ready, 1)
            split_first_rows()
            timeline(dve, slots_of)

        @block.scalar
        def _(act):
            def copy_out(e, i):
                act.wait_ge(filled, through("fills", e, i))
                src = slot_of(e)[0:KR, 0, :].bitcast(BF16)[:, 0:COLS]
                act.copy(xparts[:, events[e][1] % RING, :], src)
                act.copy(xrows[:, events[e][1] % RING, :], slot_of(e)[0:NF, 1, :]).then_inc(copied, 1)

            def square(e, i):
                act.wait_ge(filled, through("fills", e, i))
                was = user_before(e, "steps0", NSQ)
                if was is not None:
                    wait_low(act, was, i)
                if upto["steps"][e] > NBUF:
                    act.wait_ge(summed, through("steps", e, i) - NBUF)
                n = min(PAIR, CH0 - events[e][2])
                src = slot_of(e)[0:ROWS0, 0:n, :].rearrange("p a b -> p (a b)")
                act.activation(squares[0:ROWS0, sq(e), 0:n * COLS], src, ACT.Square)
                act.activation(zh[0:ROWS0, buf(e), 0:n * COLS], src, ACT.Square).then_inc(squared, 1)

            def round_high(e, i):
                act.wait_ge(multiplied, through("steps1", e, i))
                if upto["steps"][e] > NBUF:
                    act.wait_ge(summed, through("steps", e, i) - NBUF)
                src = slot_of(e).rearrange("p a b -> p (a b)") if kind_of(e) == "1" else products[:, kept(e), :]
                act.copy(zh[:, buf(e), :], src).then_inc(rounded, 1)

            def relu0(tile, i):
                a = acc[(tile + 1) % 2]
                act.wait_ge(summed, through("steps", last["0", tile], i))
                act.activation(hid[0:NEXT, tile % RING, :], a[0:NEXT], ACT.Relu)
                act.activation(hid[NEXT:P, tile % RING, :], a[0:NEXT], ACT.Relu).then_inc(hid_ready, 1)
                if tile >= QUARTERS and tile % QUARTERS == 0:
                    act.wait_ge(direct_feats, tile // QUARTERS + i)
                act.activation(maps[NEXT:P, 0, tile % QUARTERS, :], a[NEXT:P], ACT.Relu).then_inc(direct_ready, 1)

            def relu1(tile, i):
                act.wait_ge(summed, through("steps", last["1", tile], i))
                if tile >= QUARTERS and tile % QUARTERS == 0:
                    act.wait_ge(cur_feats, tile // QUARTERS + i)
                act.activation(maps[:, 1, tile % QUARTERS, :], acc[tile % 2], ACT.Relu).then_inc(cur_ready, 1)

            def copy_y(e, b, i):
                at = (b + 1) * P + i * P
                to = y_row[:, at:at + P] if isinstance(i, int) else y_row[:, bass.ds(at, P)]
                act.copy(to, slot_of(e)[0:1, 1, 0:P]).then_inc(y_ready, 1)

            def tower(e, i):
                kind, b, _ = events[e]
                act.wait_ge(filled, through("fills", e, i))
                if kind == "M":
                    for m in range(TOP1 // P):
                        ins = act.activation(act1[:, m, :], slot_of(e)[:, 0, m * P:(m + 1) * P], ACT.Relu,
                                             bias=b1[:, m:m + 1])
                    ins.then_inc(top1_act, 1)
                    copy_y(e, b - 1, i)
                if kind == "N":
                    for m in range(TOP2 // P):
                        ins = act.activation(act2[:, m, :], slot_of(e)[:, 0, m * P:(m + 1) * P], ACT.Relu,
                                             bias=b2[:, m:m + 1])
                    ins.then_inc(top2_act, 1)
                if kind == "Y":
                    copy_y(e, b, i)

            def slots_of(e, i):
                if kind_of(e) in ("1", "P", "D"):
                    round_high(e, i)
                if kind_of(e) in ("M", "N", "Y"):
                    tower(e, i)
                if kind_of(e) in ("0", "Z"):
                    square(e, i)
                if kind_of(e) == "T":
                    copy_out(e, i)
                for tile in range(TILES):
                    if last["0", tile] + (RELU_LAG if last["0", tile] >= head else HEAD_RELU_LAG) == e:
                        relu0(tile, i)
                    if last["1", tile] + RELU_LAG == e:
                        relu1(tile, i)

            act.wait_ge(sel_loaded, 32)
            act.activation(warm[:], eye_f[:, 0:1], ACT.Square)
            act.wait_ge(w_ready, 1)
            act.wait_ge(top_loaded, 5 * 16)
            timeline(act, slots_of)

        @block.tensor
        def _(pe):
            def third_layer(e, b, i):
                pe.wait_ge(top2_act, b + 2 + i)
                for q in range(TOP2 // P):
                    ins = pe.matmul(slot_of(e)[0:1, 1, 0:P], top3[:, q:q + 1], act2[:, q, :],
                                    start=(q == 0), stop=(q == TOP2 // P - 1))
                return ins

            def fill(e, i):
                kind, tile, c = events[e]
                was = user_before(e, "slots", SLOTS)
                if was is not None:
                    of, b = events[was][:2]
                    if of == "T":
                        pe.wait_ge(copied, through("copies", was, i))
                    elif of in LAYER0:
                        pe.wait_ge(squared, through("steps0", was, i))
                    elif of == "P":
                        pe.wait_ge(multiplied, through("steps1", was, i))
                    elif of == "M":
                        pe.wait_ge(y_ready, b + 1 + i)
                    elif of == "N":
                        pe.wait_ge(top2_act, b + 2 + i)
                    else:
                        pe.wait_ge(low_v, through("low_v", was, i))
                to = slot_of(e)
                if kind == "Y":
                    third_layer(e, tile, i).then_inc(filled, 1)
                    return
                if kind == "M":
                    third_layer(e, tile - 1, i)
                    pe.wait_ge(dense_loaded, 16 * (tile + 1) + i * 16)
                    pe.wait_ge(direct_feats, tile + 1 + i)
                    pe.wait_ge(cur_feats, tile + 1 + i)
                    for m in range(TOP1 // P):
                        for q, f in enumerate((feat_c, feat_d)):
                            ins = pe.matmul(to[:, 0, m * P:(m + 1) * P], top1[:, q, m * P:(m + 1) * P], f[:],
                                            start=(q == 0), stop=(q == 1))
                    ins.then_inc(filled, 1)
                    return
                if kind == "N":
                    pe.wait_ge(top1_act, tile + 1 + i)
                    for m in range(TOP2 // P):
                        for q in range(TOP1 // P):
                            ins = pe.matmul(to[:, 0, m * P:(m + 1) * P], top2[:, q, m * P:(m + 1) * P], act1[:, q, :],
                                            start=(q == 0), stop=(q == TOP1 // P - 1))
                    ins.then_inc(filled, 1)
                    return
                if kind == "T":
                    pe.wait_ge(split, 4 * (tile // QUARTERS) + 4 + i * 4)
                    flat = to[0:KR, 0, :].bitcast(BF16)
                    for d in range(DT):
                        src = parts[:, tile % QUARTERS * DT + d, :, :].rearrange("p r f -> p (r f)")
                        pe.transpose(flat[:, d * P:(d + 1) * P], src, eye[:])
                    for d in range(DT):
                        ins = pe.transpose(to[0:NF, 1, d * P:(d + 1) * P],
                                           rows_kept[:, tile % QUARTERS * DT + d, :], eye_f[:])
                    ins.then_inc(filled, 1)
                    return
                if kind in LAYER0 and c == 0:
                    pe.wait_ge(copied, through("copies", first["T", tile], i))
                m, s, end = (ROWS0, c, CH0) if kind in LAYER0 else (P, CH0 + c, SELS)
                for n in range(min(PAIR, end - s)):
                    ins = pe.matmul(to[0:m, n, :], sel[:, s + n, 0:m], xparts[:, tile % RING, :], start=True, stop=True)
                ins.then_inc(filled, 1)

            def product(e, i, low):
                kind, tile, c = events[e]
                k = buf(e)
                r, w, end = (ROWS0, c, CH0) if kind in LAYER0 else (P, CH0 + c, SELS)
                a = acc[(tile + 1) % 2] if kind in LAYER0 else acc[tile % 2]
                chunks = range(min(PAIR, end - w))
                if low:
                    wait_low(pe, e, i)
                    for n in chunks:
                        ins = pe.matmul(a, wh[0:r, w + n, :], zl[0:r, k, n * COLS:(n + 1) * COLS],
                                        start=False, stop=(w + n == end - 1))
                    ins.then_inc(summed, 1)
                    return
                if c == 0 and kind in LAYER0 and tile == 2:
                    pe.wait_ge(direct_ready, 1)
                if c == 0 and kind in LAYER0 and tile >= 3:
                    pe.wait_ge(cur_ready, tile - 2 + i * QUARTERS)
                if c == 0 and kind in LAYER1:
                    pe.wait_ge(direct_ready, min(tile + 2, TILES) + i * QUARTERS)
                if kind in LAYER0:
                    pe.wait_ge(squared, through("steps0", e, i))
                else:
                    pe.wait_ge(rounded, through("steps1", e, i))
                for n in chunks:
                    for w_ in (wh, wl):
                        pe.matmul(a, w_[0:r, w + n, :], zh[0:r, k, n * COLS:(n + 1) * COLS],
                                  start=(c == 0 and n == 0 and w_ is wh), stop=False)

            def slots_of(e, i):
                if kind_of(e) in tuple(LAYER0 + LAYER1):
                    product(e, i, low=False)
                if kind_of(e + LOOK) in tuple("T1P" + LAYER0 + TOWER):
                    fill(e + LOOK, i)
                if kind_of(e - PE_LOW_LAG) in tuple(LAYER0 + LAYER1):
                    product(e - PE_LOW_LAG, i, low=True)

            pe.wait_ge(setup_v, 3)
            for c in range(CH0):
                ins = pe.matmul(acc[0][0:FIELDS, 0:MAPS], fold[:, c, :], stage_w0a[:, c * MAPS:(c + 1) * MAPS],
                                start=(c == 0), stop=(c == CH0 - 1))
            ins.then_inc(folded, 1)
            pe.wait_ge(sel_ready, 1)
            pe.wait_ge(split_most, 4)
            pe.wait_ge(w_ready, 1)
            pe.wait_ge(top_loaded, 5 * 16)
            timeline(pe, slots_of)


def kernel(**inputs):
    import concourse.bacc as bacc
    from concourse.bass_utils import run_bass_kernel_spmd

    nc = bacc.Bacc("TRN2", target_bir_lowering=False, num_devices=1)
    arrays = {}

    def given(name, a):
        a = np.ascontiguousarray(a)
        arrays[name] = a
        return nc.dram_tensor(name, a.shape, mybir.dt.from_np(a.dtype), kind="ExternalInput").ap()

    def rows_of(w, index):
        w = np.concatenate([w, np.zeros((1, w.shape[1]), w.dtype)])
        return w[index].reshape(index.shape[0], -1)

    w0 = np.asarray(inputs["L0_rec_W0"])
    w1 = np.asarray(inputs["L0_rec_W1"])
    a, b = pairs()
    w1_at = np.arange(CH1)[None, :] * P + np.arange(P)[:, None]
    w1_at[w1_at >= FIELDS * NEXT] = -1
    t1 = np.asarray(inputs["W_top1"])
    top1 = np.zeros((P, 2, TOP1), t1.dtype)
    top1[:, 0] = t1[NEXT:NEXT + MAPS]
    top1[NEXT:, 1] = t1[0:NEXT]
    top1[0:DENSE, 1] = t1[NEXT + MAPS:]
    args = [
        given("ids_dram", np.asarray(inputs["ids"]).reshape(BLOCKS, P, FIELDS)),
        [given(f"tbl_{f}_dram", np.asarray(inputs[f"tbl_{f}"])) for f in range(FIELDS)],
        given("sel_dram", selections().reshape(PARTS * FIELDS, SELS * P)),
        given("fold_dram", own_squares()),
        given("w0a_dram", rows_of(w0, a)),
        given("w0b_dram", rows_of(w0, b)),
        given("w1_dram", rows_of(w1, w1_at)),
        given("dense_dram", np.asarray(inputs["dense_ctx"]).reshape(BLOCKS, P, DENSE).transpose(0, 2, 1)),
        given("top1_dram", top1),
        given("b1_dram", np.asarray(inputs["b_top1"]).reshape(-1, P).T),
        given("top2_dram", np.asarray(inputs["W_top2"]).reshape(-1, P, TOP2).transpose(1, 0, 2)),
        given("b2_dram", np.asarray(inputs["b_top2"]).reshape(-1, P).T),
        given("top3_dram", np.asarray(inputs["W_top3"]).reshape(-1, P).T),
        given("eye_dram", np.eye(P, dtype=np.float32)),
        nc.dram_tensor("y_dram", (1, BATCH), F32, kind="ExternalOutput").ap(),
    ]
    build(nc, *args)
    r = run_bass_kernel_spmd(nc, [arrays], core_ids=[0])
    return r.results[0]["y_dram"].reshape(BATCH, 1)
```
